# Optimizing a Trainium2 kernel written in Bass

```python
import numpy as np
import jax
import jax.numpy as jnp

def _softmax(x, axis=-1):
    return jax.nn.softmax(x, axis=axis)

def _gelu(x):
    return jax.nn.gelu(x, approximate=True)

def _silu(x):
    return jax.nn.silu(x)

def _sigmoid(x):
    return jax.nn.sigmoid(x)

def _layernorm(x, axis=-1, eps=1e-05):
    m = jnp.mean(x, axis=axis, keepdims=True)
    v = jnp.var(x, axis=axis, keepdims=True)
    return (x - m) / jnp.sqrt(v + eps)

def _scatter_add(tgt, idx, src, axis=0):
    return tgt.at[idx].add(src)

def _segment_sum(src, seg, n):
    return jax.ops.segment_sum(src, seg, n)
kernel_name = 'mk_gnn_preln_d2_gnn_r32_faaf92'

def setup_inputs(seed: int=0):
    np.random.seed(seed)
    _w = jnp.asarray

    def _rec_inputs():
        import jax
        import jax.numpy as jnp
        _gk = jax.random.key(seed)
        x = -1.686e-05 + 1 * jax.random.normal(jax.random.fold_in(_gk, 1), (50000, 160), jnp.float32)
        src = jax.random.randint(jax.random.fold_in(_gk, 2), (50000,), 0, 50000, jnp.int32)
        dst = jax.random.randint(jax.random.fold_in(_gk, 3), (50000,), 0, 50000, jnp.int32)
        _o = jnp.argsort(dst, stable=True)
        src = src[_o]
        dst = dst[_o]
        edge_attr_10 = jax.random.uniform(jax.random.fold_in(_gk, 12), (50000, 10), jnp.float32, 0.0, 1)
        edge_attr_4 = -0.000107899 + 1.00008 * jax.random.normal(jax.random.fold_in(_gk, 13), (50000, 4), jnp.float32)
        edge_attr_8 = jax.random.uniform(jax.random.fold_in(_gk, 14), (50000, 8), jnp.float32, 0.0, 1)
        node_vec1 = jax.random.uniform(jax.random.fold_in(_gk, 16), (50000, 1), jnp.float32, 0.0, 1)
        return (x, src, dst, edge_attr_10, edge_attr_4, edge_attr_8, node_vec1)
    x, src, dst, edge_attr_10, edge_attr_4, edge_attr_8, node_vec1 = _rec_inputs()

    def _L0_gnn_setup():
        import jax, jax.numpy as jnp
        import numpy as np
        N = 50000
        E = 25000
        MUL0 = 64
        MUL1 = 32
        NB = 8
        HID = 64
        WNUM = MUL0 + MUL0 + MUL1 + MUL1
        D_IN = MUL0 + 3 * MUL1
        AVG_DEG = E / N
        key = jax.random.key(seed)
        ks = jax.random.split(key, 16)
        p = lambda i, s: jax.random.normal(ks[i], s, jnp.float32)
        return {'node_features': p(0, (N, D_IN)), 'edge_sh': p(1, (E, 4)), 'edge_embed': jax.random.uniform(ks[2], (E, NB), jnp.float32), 'W1_s': p(3, (MUL0, MUL0)), 'W1_v': p(4, (MUL1, MUL1)), 'fc_w1': p(5, (NB, HID)), 'fc_b1': jnp.zeros((HID,), jnp.float32), 'fc_w2': p(6, (HID, WNUM)) * 0.1, 'fc_b2': jnp.zeros((WNUM,), jnp.float32), 'W2_s': p(7, (96, 96)), 'W2_v': p(8, (96, MUL1)), 'Wsc_s': p(9, (MUL0, 96)), 'Wsc_v': p(10, (MUL1, MUL1)), 'edge_index': jax.random.randint(ks[11], (2, E), 0, N)}
    _L0_gnn_all = _L0_gnn_setup()
    _L0_gnn_in = {k: v for k, v in _L0_gnn_all.items() if k in ('W1_s', 'W1_v', 'fc_w1', 'fc_b1', 'fc_w2', 'fc_b2', 'W2_s', 'W2_v', 'Wsc_s', 'Wsc_v')}
    del _L0_gnn_all

    def _L1_gnn_setup():
        import jax, jax.numpy as jnp
        import numpy as np
        N_NODES = 50000
        N_EDGES = 25000
        MUL0, MUL1 = (64, 32)
        N_BASIS, N_RADIAL = (10, 100)
        W_NUMEL = 192
        NUM_NEIGHBORS = 16.0
        INV_SQRT3 = np.float32(1.0 / np.sqrt(3.0))
        RELU_GAIN = np.float32(np.sqrt(2.0))
        FAN_L2 = np.float32(np.sqrt(MUL0 + MUL1))

        def _fctp_scalar_attr(x0, x1, a, W0, W1):
            o0 = x0 @ W0 * a * (1.0 / np.sqrt(W0.shape[0]))
            o1 = jnp.einsum('nud,uw->nwd', x1, W1) * a[..., None] * (1.0 / np.sqrt(W1.shape[0]))
            return (o0, o1)
        key = jax.random.key(seed)
        ks = jax.random.split(key, 16)
        return {'node_input': jax.random.normal(ks[0], (N_NODES, MUL0 + 3 * MUL1), jnp.float32), 'node_attr': jnp.ones((N_NODES, 1), jnp.float32), 'edge_attr': jax.random.normal(ks[1], (N_EDGES, 4), jnp.float32), 'edge_length_embedded': jax.random.uniform(ks[2], (N_EDGES, N_BASIS), dtype=jnp.float32), 'W_si0': jax.random.normal(ks[3], (MUL0, MUL0), jnp.float32), 'W_si1': jax.random.normal(ks[4], (MUL1, MUL1), jnp.float32), 'W_l1_0': jax.random.normal(ks[5], (MUL0, MUL0), jnp.float32), 'W_l1_1': jax.random.normal(ks[6], (MUL1, MUL1), jnp.float32), 'W_l2_00': jax.random.normal(ks[7], (MUL0, MUL0), jnp.float32), 'W_l2_10': jax.random.normal(ks[8], (MUL1, MUL0), jnp.float32), 'W_l2_01': jax.random.normal(ks[9], (MUL0, MUL1), jnp.float32), 'W_l2_11': jax.random.normal(ks[10], (MUL1, MUL1), jnp.float32), 'W_fc1': jax.random.normal(ks[11], (N_BASIS, N_RADIAL), jnp.float32), 'W_fc2': jax.random.normal(ks[12], (N_RADIAL, W_NUMEL), jnp.float32), 'edge_src': jax.random.randint(ks[13], (N_EDGES,), 0, N_NODES), 'edge_dst': jax.random.randint(ks[14], (N_EDGES,), 0, N_NODES)}
    _L1_gnn_all = _L1_gnn_setup()
    _L1_gnn_in = {k: v for k, v in _L1_gnn_all.items() if k in ('W_si0', 'W_si1', 'W_l1_0', 'W_l1_1', 'W_l2_00', 'W_l2_10', 'W_l2_01', 'W_l2_11', 'W_fc1', 'W_fc2')}
    del _L1_gnn_all
    return {'x': x, 'src': src, 'dst': dst, 'edge_attr_10': edge_attr_10, 'edge_attr_4': edge_attr_4, 'edge_attr_8': edge_attr_8, 'node_vec1': node_vec1, 'L0_gnn_W1_s': _L0_gnn_in['W1_s'], 'L0_gnn_W1_v': _L0_gnn_in['W1_v'], 'L0_gnn_fc_w1': _L0_gnn_in['fc_w1'], 'L0_gnn_fc_b1': _L0_gnn_in['fc_b1'], 'L0_gnn_fc_w2': _L0_gnn_in['fc_w2'], 'L0_gnn_fc_b2': _L0_gnn_in['fc_b2'], 'L0_gnn_W2_s': _L0_gnn_in['W2_s'], 'L0_gnn_W2_v': _L0_gnn_in['W2_v'], 'L0_gnn_Wsc_s': _L0_gnn_in['Wsc_s'], 'L0_gnn_Wsc_v': _L0_gnn_in['Wsc_v'], 'L1_gnn_W_si0': _L1_gnn_in['W_si0'], 'L1_gnn_W_si1': _L1_gnn_in['W_si1'], 'L1_gnn_W_l1_0': _L1_gnn_in['W_l1_0'], 'L1_gnn_W_l1_1': _L1_gnn_in['W_l1_1'], 'L1_gnn_W_l2_00': _L1_gnn_in['W_l2_00'], 'L1_gnn_W_l2_10': _L1_gnn_in['W_l2_10'], 'L1_gnn_W_l2_01': _L1_gnn_in['W_l2_01'], 'L1_gnn_W_l2_11': _L1_gnn_in['W_l2_11'], 'L1_gnn_W_fc1': _L1_gnn_in['W_fc1'], 'L1_gnn_W_fc2': _L1_gnn_in['W_fc2']}

def reference(x, src, dst, edge_attr_10, edge_attr_4, edge_attr_8, node_vec1, L0_gnn_W1_s, L0_gnn_W1_v, L0_gnn_fc_w1, L0_gnn_fc_b1, L0_gnn_fc_w2, L0_gnn_fc_b2, L0_gnn_W2_s, L0_gnn_W2_v, L0_gnn_Wsc_s, L0_gnn_Wsc_v, L1_gnn_W_si0, L1_gnn_W_si1, L1_gnn_W_l1_0, L1_gnn_W_l1_1, L1_gnn_W_l2_00, L1_gnn_W_l2_10, L1_gnn_W_l2_01, L1_gnn_W_l2_11, L1_gnn_W_fc1, L1_gnn_W_fc2):
    import jax
    import jax.numpy as jnp

    def _L0_gnn_ref(node_features, edge_sh, edge_embed, W1_s, W1_v, fc_w1, fc_b1, fc_w2, fc_b2, W2_s, W2_v, Wsc_s, Wsc_v, edge_index):
        import jax, jax.numpy as jnp
        import numpy as np
        N = 50000
        E = 25000
        MUL0 = 64
        MUL1 = 32
        NB = 8
        HID = 64
        WNUM = MUL0 + MUL0 + MUL1 + MUL1
        D_IN = MUL0 + 3 * MUL1
        AVG_DEG = E / N
        n = node_features.shape[0]
        s = node_features[:, :MUL0]
        v = node_features[:, MUL0:].reshape(n, MUL1, 3)
        xs = s @ W1_s / np.sqrt(MUL0)
        xv = jnp.einsum('nmc,mk->nkc', v, W1_v) / np.sqrt(MUL1)
        src, dst = (edge_index[0], edge_index[1])
        sh0 = edge_sh[:, 0]
        sh1 = edge_sh[:, 1:4]
        w = jax.nn.silu(edge_embed @ fc_w1 + fc_b1) @ fc_w2 + fc_b2
        w_ss = w[:, :MUL0]
        w_sv = w[:, MUL0:2 * MUL0]
        w_vs = w[:, 2 * MUL0:2 * MUL0 + MUL1]
        w_vv = w[:, 2 * MUL0 + MUL1:]
        xs_e = xs[src]
        xv_e = xv[src]
        m0_a = w_ss * xs_e * sh0[:, None]
        m1_a = (w_sv * xs_e)[:, :, None] * sh1[:, None, :]
        m1_b = w_vs[:, :, None] * xv_e * sh0[:, None, None]
        m0_b = w_vv * jnp.einsum('emc,ec->em', xv_e, sh1) / np.sqrt(3.0)
        msg = jnp.concatenate([m0_a, m0_b, m1_a.reshape(-1, MUL0 * 3), m1_b.reshape(-1, MUL1 * 3)], axis=1)
        agg = jax.ops.segment_sum(msg, dst, num_segments=n) / np.sqrt(AVG_DEG)
        agg_s = agg[:, :96]
        agg_v = agg[:, 96:].reshape(n, 96, 3)
        out_s = agg_s @ W2_s / np.sqrt(96.0)
        out_v = jnp.einsum('nmc,mk->nkc', agg_v, W2_v) / np.sqrt(96.0)
        out_s = out_s + s @ Wsc_s / np.sqrt(MUL0)
        out_v = out_v + jnp.einsum('nmc,mk->nkc', v, Wsc_v) / np.sqrt(MUL1)
        scalars = jax.nn.silu(out_s[:, :MUL0])
        gates = jax.nn.silu(out_s[:, MUL0:MUL0 + MUL1])
        gated = out_v * gates[:, :, None]
        feats = jnp.concatenate([scalars, gated.reshape(n, MUL1 * 3)], axis=1)
        return node_features + feats

    def _L1_gnn_ref(node_input, node_attr, edge_src, edge_dst, edge_attr, edge_length_embedded, W_si0, W_si1, W_l1_0, W_l1_1, W_l2_00, W_l2_10, W_l2_01, W_l2_11, W_fc1, W_fc2):
        import jax, jax.numpy as jnp
        import numpy as np
        N_NODES = 50000
        N_EDGES = 25000
        MUL0, MUL1 = (64, 32)
        N_BASIS, N_RADIAL = (10, 100)
        W_NUMEL = 192
        NUM_NEIGHBORS = 16.0
        INV_SQRT3 = np.float32(1.0 / np.sqrt(3.0))
        RELU_GAIN = np.float32(np.sqrt(2.0))
        FAN_L2 = np.float32(np.sqrt(MUL0 + MUL1))

        def _fctp_scalar_attr(x0, x1, a, W0, W1):
            o0 = x0 @ W0 * a * (1.0 / np.sqrt(W0.shape[0]))
            o1 = jnp.einsum('nud,uw->nwd', x1, W1) * a[..., None] * (1.0 / np.sqrt(W1.shape[0]))
            return (o0, o1)
        N = node_input.shape[0]
        x0 = node_input[:, :MUL0]
        x1 = node_input[:, MUL0:].reshape(N, MUL1, 3)
        a = node_attr
        h = jax.nn.relu(edge_length_embedded @ W_fc1 * (1.0 / np.sqrt(N_BASIS))) * RELU_GAIN
        w = h @ W_fc2 * (1.0 / np.sqrt(N_RADIAL))
        w0, w1, w2, w3 = (w[:, :64], w[:, 64:128], w[:, 128:160], w[:, 160:192])
        si0, si1 = _fctp_scalar_attr(x0, x1, a, W_si0, W_si1)
        l0, l1 = _fctp_scalar_attr(x0, x1, a, W_l1_0, W_l1_1)
        y0 = l0[edge_src]
        y1 = l1[edge_src]
        e0 = edge_attr[:, :1]
        e1 = edge_attr[:, 1:4]
        m0 = w0 * y0 * e0
        m1 = (w1 * y0)[:, :, None] * e1[:, None, :]
        m2 = (w2 * e0)[:, :, None] * y1
        m3 = w3 * jnp.einsum('eud,ed->eu', y1, e1) * INV_SQRT3
        inv = np.float32(1.0 / np.sqrt(NUM_NEIGHBORS))
        s0 = jax.ops.segment_sum(m0, edge_dst, num_segments=N) * inv
        s1 = jax.ops.segment_sum(m1, edge_dst, num_segments=N) * inv
        s2 = jax.ops.segment_sum(m2, edge_dst, num_segments=N) * inv
        s3 = jax.ops.segment_sum(m3, edge_dst, num_segments=N) * inv
        o0 = (s0 @ W_l2_00 + s3 @ W_l2_10) * a / FAN_L2
        o1 = (jnp.einsum('nud,uw->nwd', s1, W_l2_01) + jnp.einsum('nud,uw->nwd', s2, W_l2_11)) * a[..., None] / FAN_L2
        out0 = si0 + 0.5 * o0
        out1 = si1 + 0.5 * o1
        return jnp.concatenate([out0, out1.reshape(N, 3 * MUL1)], axis=1)
    edge_index = jnp.stack([src, dst])
    h = jnp.maximum(_layernorm(x, axis=-1), 0.0)
    x = x + _L0_gnn_ref(h, edge_attr_4, edge_attr_8, L0_gnn_W1_s, L0_gnn_W1_v, L0_gnn_fc_w1, L0_gnn_fc_b1, L0_gnn_fc_w2, L0_gnn_fc_b2, L0_gnn_W2_s, L0_gnn_W2_v, L0_gnn_Wsc_s, L0_gnn_Wsc_v, edge_index)
    h = jnp.maximum(_layernorm(x, axis=-1), 0.0)
    x = x + _L1_gnn_ref(h, node_vec1, src, dst, edge_attr_4, edge_attr_10, L1_gnn_W_si0, L1_gnn_W_si1, L1_gnn_W_l1_0, L1_gnn_W_l1_1, L1_gnn_W_l2_00, L1_gnn_W_l2_10, L1_gnn_W_l2_01, L1_gnn_W_l2_11, L1_gnn_W_fc1, L1_gnn_W_fc2)
    return x

_drawn_inputs = setup_inputs


def setup_inputs(seed=0):
    import zlib

    import numpy as np

    out = dict(_drawn_inputs(seed))
    spreads = {'L0_gnn_fc_b1': (0.0, 0.427), 'L0_gnn_fc_b2': (0.0, 0.1)}
    factors = {'edge_attr_10': 8.0,
     'L1_gnn_W_l1_0': 7.248,
     'L1_gnn_W_l1_1': 8.0,
     'L1_gnn_W_l2_00': 8.0,
     'L1_gnn_W_l2_10': 8.0,
     'L1_gnn_W_l2_01': 8.0,
     'L1_gnn_W_l2_11': 8.0,
     'L1_gnn_W_fc1': 7.33,
     'L1_gnn_W_fc2': 6.395,
     'L1_gnn_W_si0': 64.0,
     'L1_gnn_W_si1': 64.0}
    for name, (base, spread) in spreads.items():
        noise = np.random.default_rng([zlib.crc32(name.encode()), seed]).standard_normal(out[name].shape)
        drawn = base * np.exp(spread * noise) if base else spread * noise
        out[name] = jnp.asarray(drawn.astype(out[name].dtype))
    for name, factor in factors.items():
        out[name] = (out[name] * factor).astype(out[name].dtype)
    return out
```

```python
from contextlib import ExitStack

import numpy as np

import concourse.bass as bass
from concourse import mybir

F32 = mybir.dt.float32
I32 = mybir.dt.int32
ALU = mybir.AluOpType
ACT = mybir.ActivationFunctionType
AX = mybir.AxisListType

N = 50000
E = 50000
P = 128
MUL0, MUL1 = 64, 32
VEC = 3 * MUL1
D = MUL0 + VEC
DA = D + 1
SW = MUL0 + MUL1
WN = 2 * MUL0 + 2 * MUL1
NT = 100
TILES = N // NT
PAIR = 2
NB = TILES // PAIR
RING = 6
ROW = 392
EP = P * ROW
CHUNKS = EP // P
REC = 6
LISTED = 512
TC = LISTED // P
EPS = 1e-5

AHEAD, BEHIND = 2, 6
PEEL = 8
LOOPS = (NB - AHEAD - PEEL) // RING
LAST = PEEL + LOOPS * RING


class Turn:

    def __init__(self, n, m, uses, slot, half, tiles, serial):
        self.n, self.m, self.uses, self.slot, self.half, self.tiles, self.serial = n, m, uses, slot, half, tiles, serial

    def freed(self, depth):
        return self.n if self.serial else self.n - depth + 1

    def freed_m(self, depth):
        return self.m if self.serial else self.m - depth + 1


def main_turn(b, i=None):
    if i is None:
        if not 0 <= b < NB:
            return None
        return Turn(b, b, b // RING, b % RING, b % 2, PAIR, False)
    return Turn(i * RING + b, i * RING + b, i + b // RING, b % RING, b % 2, PAIR, False)


def run_steps(eng, step, ahead_of=None):
    for s in range(PEEL):
        step(lambda k: main_turn(s - k))
    with eng.Fori(0, LOOPS) as i:
        if ahead_of:
            ahead_of(i)
        for j in range(RING):
            step(lambda k: main_turn(PEEL + j - k, i))
    for s in range(LAST, NB + BEHIND + 1):
        step(lambda k: main_turn(s - k))


def hold(eng, sem, count):
    if isinstance(count, int) and count <= 0:
        return
    eng.wait_ge(sem, count)


def wait_apart(eng, sem, count, passed):
    if isinstance(count, int) and count <= 0:
        return
    eng.wait_ge(sem, count)
    eng.sem_inc(passed, 1)


def build(nc, x, sd, dst_rows, dst_next, row_last, sh, ee, wts, out):
    xmid = nc.dram_tensor("xmid", [N, DA], F32, kind="Internal").ap()
    start_tab = nc.dram_tensor("start_tab", [1, LISTED], I32, kind="Internal").ap()
    edge_rec = nc.dram_tensor("edge_rec", [EP, REC], I32, kind="Internal").ap()
    long_tab = nc.dram_tensor("long_tab", [LISTED, 4], I32, kind="Internal").ap()
    long_num = nc.dram_tensor("long_num", [1, 1], I32, kind="Internal").ap()

    with ExitStack() as ctx:
        def sb(name, shape, dt=F32):
            return ctx.enter_context(nc.sbuf_tensor(name, shape, dt))

        def ps(name, shape, dt=F32):
            return ctx.enter_context(nc.psum_tensor(name, shape, dt))

        def sem(name):
            return ctx.enter_context(nc.semaphore(name))

        ident = sb("ident", [P, P])
        iota_n = sb("iota_n", [P, NT])
        neghalf = sb("neghalf", [P, 2 * PAIR])
        zeros = sb("zeros", [P, 4 * P])

        w = {name: sb("w_" + name, list(ap.shape)) for name, ap in wts.items()}

        S1 = RING + 1
        win = sb("win", [P, S1, PAIR, REC], I32)
        starts = sb("starts", [1, LISTED], I32)
        ee_sb = sb("ee_sb", [16, S1, PAIR, P])
        xg = sb("xg", [P, S1, PAIR, DA])
        xn = sb("xn", [P, S1, PAIR, DA])
        xo = sb("xo", [P, S1, PAIR, DA])
        st = sb("st", [P, 2, 2, PAIR, 6])
        mv = sb("mv", [P, 2, 2, PAIR, 2])
        ve = sb("ve", [P, 2, PAIR])
        rs = sb("rs", [P, 2, 2, PAIR])
        nmr = sb("nmr", [P, 2, PAIR])
        ra = sb("ra", [P, PAIR])
        he = sb("he", [P, 2, PAIR, D])
        hn = sb("hn", [P, 2, PAIR, DA])
        she = sb("she", [P, S1, PAIR, 4])
        hT = sb("hT", [SW, S1, PAIR, 4, P])
        hid = sb("hid", [P, 2, PAIR, P])
        xw_sb = sb("xw_sb", [P, 2, PAIR, D + WN])
        xs0 = sb("xs0", [P, 2, PAIR, D])
        pw = sb("pw", [P, PAIR, MUL0])
        qv = sb("qv", [P, PAIR, 3, MUL1])
        tv = sb("tv", [P, 2, PAIR, MUL1])
        msg = sb("msg", [P, 2, PAIR, 4, SW])
        drel = sb("drel", [P, PAIR])
        base = sb("base", [P, PAIR])
        base_i = sb("base_i", [P, 1], I32)
        sel = sb("sel", [P, 2, PAIR, NT])
        aggT = sb("aggT", [SW, 2, PAIR, 4, NT])
        fe = sb("fe", [P, 2, PAIR, 2 * SW + 1])

        hT_ps = ps("hT_ps", [P, PAIR, 4, P])
        hid_ps = ps("hid_ps", [P, 512])
        xw_ps = ps("xw_ps", [P, PAIR, 512])
        agg_ps = ps("agg_ps", [P, PAIR, 512])
        out_ps = ps("out_ps", [P, 512])

        setup(nc, ctx, sb, sem, dict(locals()))

        for layer, (src_rows, dst_dram) in enumerate([(x, xmid), (xmid, out)]):
            with ExitStack() as lctx:
                one_layer(nc, lctx, layer, src_rows, dst_dram, dict(locals()))


def setup(nc, ctx, sb, sem, v):
    w, wts = v["w"], v["wts"]
    ident, iota_n, neghalf, zeros = v["ident"], v["iota_n"], v["neghalf"], v["zeros"]
    xn, hn, fe, ee_sb, hid = v["xn"], v["hn"], v["fe"], v["ee_sb"], v["hid"]
    dst_rows, dst_next, row_last, sd = v["dst_rows"], v["dst_next"], v["row_last"], v["sd"]
    start_tab, long_tab, long_num = v["start_tab"], v["long_tab"], v["long_num"]
    sh, edge_rec, starts = v["sh"], v["edge_rec"], v["starts"]
    agg_ps = v["agg_ps"]

    iv = sb("iv", [P, 4 * P], I32)
    step_i = sb("step_i", [P, CHUNKS], I32)
    steps = sb("steps", [P, CHUNKS])
    tile_i = sb("tile_i", [P, TC], I32)
    bound = sb("bound", [P, 2 * TC])
    last_i = sb("last_i", [P, P], I32)
    last_f = sb("last_f", [P, P])
    d_i = sb("d_i", [P, 2, ROW], I32)
    d_f = sb("d_f", [P, 2, ROW])
    ones = sb("ones", [P, P])
    upper = sb("upper", [P, P])
    scr = sb("scr", [P, ROW])
    full = sb("full", [P, 2 * TC])
    full_i = sb("full_i", [P, 2 * TC], I32)
    found_i = sb("found_i", [P, 2 * TC, ROW], I32)
    found = sb("found", [P, ROW])
    part = sb("part", [P, 2 * TC])
    low = sb("low", [P, 2 * TC])
    bad = sb("bad", [P, 1])
    ok = sb("ok", [P, 1])
    num = sb("num", [P, TC])
    chunks = sb("chunks", [P, TC])
    flag = sb("flag", [P, TC])
    pos = sb("pos", [P, TC])
    run = sb("run", [P, TC + 1])
    rec = sb("rec", [P, TC, 4])
    rec_i = sb("rec_i", [P, TC, 4], I32)
    pos_i = sb("pos_i", [P, TC], I32)
    tot_i = sb("tot_i", [P, 1], I32)
    dflt = sb("dflt", [1, 4], I32)

    raw_sd = sb("raw_sd", [P, ROW, 2], I32)
    raw_sh = sb("raw_sh", [P, ROW, 4])
    recs = sb("recs", [P, ROW, REC], I32)

    s_raw = sem("s_raw")
    s_recs = sem("s_recs")
    s_starts = sem("s_starts")
    s_iota = sem("s_iota")
    s_w = sem("s_w")
    s_tab = sem("s_tab")
    s_vec = sem("s_vec")
    s_full = sem("s_full")
    s_found = sem("s_found")
    s_cnt = sem("s_cnt")
    s_pref = sem("s_pref")
    s_rec = sem("s_rec")
    s_dflt = sem("s_dflt")
    s_list = sem("s_list")
    s_scat = sem("s_scat")

    nw = len(w)
    with nc.Block() as block:
        @block.sync
        def _(sp):
            sp.dma_start(last_i[:, :], row_last.partition_broadcast(P)).then_inc(s_tab, 16)
            sp.dma_start(d_i[:, 0, :], dst_rows).then_inc(s_tab, 16)
            sp.dma_start(d_i[:, 1, :], dst_next).then_inc(s_tab, 16)
            sp.dma_start(raw_sd[:, :, :], sd.rearrange("(p r) c -> p r c", p=P)).then_inc(s_raw, 16)
            sp.dma_start(raw_sh[:, :, :], sh.rearrange("(p r) c -> p r c", p=P)).then_inc(s_raw, 16)
            for name in w:
                sp.dma_start(w[name][:, :], wts[name]).then_inc(s_w, 16)
            sp.wait_ge(s_dflt, 1)
            sp.dma_start(long_tab[0:1, :], dflt[:, :]).then_inc(s_list, 16)
            sp.wait_ge(s_rec, 1)
            for k in range(TC):
                sp.dma_start(start_tab[:, k * P:(k + 1) * P].rearrange("a p -> p a"), rec_i[:, k, 1:2]).then_inc(s_list, 16)
            sp.dma_start(long_num, tot_i[0:1, :]).then_inc(s_list, 16)
            sp.wait_ge(s_recs, 1)
            sp.dma_start(edge_rec.rearrange("(p r) c -> p r c", p=P), recs[:, :, :]).then_inc(s_list, 16)
            sp.wait_ge(s_list, 16 * (3 + TC))
            sp.wait_ge(s_scat, 16 * TC)
            sp.dma_start(starts[:, :], start_tab).then_inc(s_starts, 16)
            sp.wait_ge(s_starts, 16)

        @block.gpsimd
        def _(pool):
            pool.iota(iv[:, 0:P], pattern=[[1, P]], base=0, channel_multiplier=-1).then_inc(s_iota, 1)
            pool.iota(iv[:, P:P + NT], pattern=[[1, NT]], base=0, channel_multiplier=0).then_inc(s_iota, 1)
            pool.iota(step_i[:, :], pattern=[[P, CHUNKS]], base=0, channel_multiplier=0).then_inc(s_iota, 1)
            pool.iota(tile_i[:, :], pattern=[[P, TC]], base=0, channel_multiplier=1).then_inc(s_iota, 1)
            pool.memset(neghalf[:, :], -0.5)
            pool.memset(zeros[:, :], 0.0)
            pool.memset(xn[:, :, :, :], 0.0)
            pool.memset(hn[:, :, :, :], 0.0)
            pool.memset(fe[:, :, :, :], 0.0)
            pool.memset(ee_sb[:, :, :, :], 1.0)
            pool.memset(hid[:, :, :, :], 1.0)
            pool.memset(dflt[:, 0:2], 0)
            pool.memset(dflt[:, 2:3], 1)
            pool.memset(dflt[:, 3:4], 0).then_inc(s_dflt, 1)
            pool.wait_ge(s_full, 1)
            for k in range(2 * TC):
                pool.indirect_dma_start(out=found_i[:, k, :], out_offset=None, in_=dst_rows,
                                        in_offset=bass.IndirectOffsetOnAxis(ap=full_i[:, k:k + 1], axis=0)).then_inc(s_found, 16)
            pool.wait_ge(s_rec, 1)
            pool.wait_ge(s_list, 16 * (3 + TC))
            for k in range(TC):
                pool.indirect_dma_start(out=long_tab, out_offset=bass.IndirectOffsetOnAxis(ap=pos_i[:, k:k + 1], axis=0),
                                        in_=rec_i[:, k, :], in_offset=None,
                                        bounds_check=LISTED - 1, oob_is_err=False).then_inc(s_scat, 16)

        @block.vector
        def _(dve):
            count = [0]

            def link(ins):
                count[0] += 1
                ins.then_inc(s_vec, 1)
                dve.wait_ge(s_vec, count[0])

            dve.wait_ge(s_iota, 4)
            dve.tensor_scalar(ident[:, :], iv[:, 0:P], 0.0, None, ALU.is_equal)
            dve.tensor_scalar(upper[:, :], iv[:, 0:P], 0.0, None, ALU.is_gt)
            dve.tensor_copy(iota_n[:, :], iv[:, P:P + NT])
            dve.tensor_copy(steps[:, :], step_i[:, :])
            dve.memset(ones[:, :], 1.0)
            dve.tensor_scalar(bound[:, 0:TC], tile_i[:, :], float(NT), None, ALU.mult)
            dve.tensor_scalar(bound[:, TC:2 * TC], tile_i[:, :], float(NT), float(NT), ALU.mult, ALU.add)
            dve.wait_ge(s_tab, 48)
            dve.tensor_copy(last_f[:, :], last_i[:, :])
            link(dve.tensor_copy(d_f[:, :, :], d_i[:, :, :]))
            link(dve.tensor_tensor(scr[:, :], d_f[:, 0, :], d_f[:, 1, :], ALU.is_gt))
            link(dve.reduce_sum(bad[:, :], scr[:, :], AX.X))
            for k in range(2 * TC):
                link(dve.tensor_scalar(scr[:, 0:P], last_f[:, :], bound[:, k:k + 1], 0.0, ALU.is_lt, ALU.add,
                                       accum_out=full[:, k:k + 1]))
            link(dve.tensor_scalar(full[:, :], full[:, :], float(P - 1), None, ALU.min))
            dve.tensor_copy(full_i[:, :], full[:, :]).then_inc(s_full, 1)
            dve.wait_ge(s_raw, 32)
            dve.tensor_copy(recs[:, :, 0:2], raw_sd[:, :, :])
            dve.tensor_copy(recs[:, :, 2:REC].bitcast(F32), raw_sh[:, :, :]).then_inc(s_recs, 1)
            dve.wait_ge(s_w, 16 * nw)
            r8, r32, r3 = 1 / np.sqrt(64.0), 1 / np.sqrt(32.0), 1 / np.sqrt(3.0)
            agg0 = 1 / np.sqrt(96.0) / np.sqrt(E / 2 / N)
            agg1 = 0.25 * 0.5 / np.sqrt(96.0)
            for name, scale in (("lin_s0", r8), ("lin_v0", r32), ("sc_s0", r8), ("sc_v0", r32), ("out_s0", agg0), ("out_v0", agg0),
                                ("lin_s1", r8), ("lin_v1", r32), ("sc_s1", r8), ("sc_v1", r32), ("out_s1", agg1), ("out_v1", agg1),
                                ("fc1_1", 1 / np.sqrt(10.0))):
                dve.tensor_scalar(w[name][:, :], w[name][:, :], float(scale), None, ALU.mult)
            for name, scale in (("fc2_0", 1.0), ("fc2_1", np.sqrt(2.0) / np.sqrt(100.0))):
                a = WN - MUL1
                dve.tensor_scalar(w[name][:, 0:a], w[name][:, 0:a], float(scale), None, ALU.mult)
                dve.tensor_scalar(w[name][:, a:WN], w[name][:, a:WN], float(scale * r3), None, ALU.mult)
            dve.wait_ge(s_found, 16 * 2 * TC)
            for k in range(2 * TC):
                link(dve.tensor_copy(found[:, :], found_i[:, k, :]))
                link(dve.tensor_scalar(scr[:, :], found[:, :], bound[:, k:k + 1], 0.0, ALU.is_lt, ALU.add,
                                       accum_out=part[:, k:k + 1]))
            link(dve.scalar_tensor_tensor(out=low[:, :], in0=full[:, :], scalar=float(ROW), in1=part[:, :],
                                          op0=ALU.mult, op1=ALU.add))
            dve.wait_ge(s_cnt, 1)
            link(dve.tensor_scalar(ok[:, :], agg_ps[:, 0, 0:1], 0.0, None, ALU.is_equal))
            link(dve.tensor_scalar(low[:, :], low[:, :], ok[:, 0:1], None, ALU.mult))
            link(dve.tensor_tensor(num[:, :], low[:, TC:2 * TC], low[:, 0:TC], ALU.subtract))
            for k in range(TC):
                link(dve.tensor_scalar(scr[:, 0:CHUNKS], steps[:, :], num[:, k:k + 1], 0.0, ALU.is_lt, ALU.add,
                                       accum_out=chunks[:, k:k + 1]))
            link(dve.tensor_scalar(chunks[:, :], chunks[:, :], -float(CHUNKS), ok[:, 0:1], ALU.add, ALU.mult))
            link(dve.tensor_scalar(chunks[:, :], chunks[:, :], float(CHUNKS), None, ALU.add))
            link(dve.tensor_scalar(flag[:, :], chunks[:, :], 1.5, None, ALU.is_gt))
            link(dve.tensor_scalar(pos[:, :], bound[:, 0:TC], float(N) - 0.5, None, ALU.is_lt))
            dve.tensor_tensor(flag[:, :], flag[:, :], pos[:, :], ALU.mult).then_inc(s_cnt, 1)
            dve.wait_ge(s_pref, 1)
            link(dve.memset(run[:, 0:1], 0.0))
            for k in range(TC):
                link(dve.tensor_tensor(run[:, k + 1:k + 2], run[:, k:k + 1], agg_ps[:, 1, P + k:P + k + 1], ALU.add))
            link(dve.tensor_tensor(pos[:, :], run[:, 0:TC], agg_ps[:, 1, 0:TC], ALU.add))
            link(dve.tensor_scalar(pos[:, :], pos[:, :], -2.0 * LISTED, None, ALU.add))
            link(dve.tensor_tensor(pos[:, :], pos[:, :], flag[:, :], ALU.mult))
            link(dve.tensor_scalar(pos[:, :], pos[:, :], 2.0 * LISTED, None, ALU.add))
            dve.tensor_copy(pos_i[:, :], pos[:, :])
            link(dve.tensor_scalar(run[:, TC:TC + 1], run[:, TC:TC + 1], 1.0, None, ALU.max))
            dve.tensor_copy(tot_i[:, :], run[:, TC:TC + 1])
            dve.tensor_copy(rec[:, :, 0], tile_i[:, :])
            dve.tensor_copy(rec[:, :, 1], low[:, 0:TC])
            dve.tensor_copy(rec[:, :, 2], chunks[:, :])
            link(dve.tensor_copy(rec[:, :, 3], bound[:, 0:TC]))
            dve.tensor_copy(rec_i[:, :, :], rec[:, :, :]).then_inc(s_rec, 1)

        @block.tensor
        def _(pe):
            pe.wait_ge(s_vec, 3)
            pe.matmul(agg_ps[:, 0, 0:1], ones[:, :], bad[:, :], start=True, stop=True).then_inc(s_cnt, 1)
            pe.wait_ge(s_cnt, 2)
            pe.matmul(agg_ps[:, 1, 0:TC], upper[:, :], flag[:, :], start=True, stop=True)
            pe.matmul(agg_ps[:, 1, P:P + TC], ones[:, :], flag[:, :], start=True, stop=True).then_inc(s_pref, 1)


def one_layer(nc, lctx, layer, src_rows, dst_dram, v):
    w = {k[:-1]: t for k, t in v["w"].items() if k.endswith(str(layer))}
    ident, iota_n, neghalf, zeros = v["ident"], v["iota_n"], v["neghalf"], v["zeros"]
    win, starts, ee_sb, xg, xn, xo = v["win"], v["starts"], v["ee_sb"], v["xg"], v["xn"], v["xo"]
    st, mv, ve, rs, nmr, ra, he, hn, she = v["st"], v["mv"], v["ve"], v["rs"], v["nmr"], v["ra"], v["he"], v["hn"], v["she"]
    hT, hid, xw_sb, xs0, pw, qv, tv, msg = v["hT"], v["hid"], v["xw_sb"], v["xs0"], v["pw"], v["qv"], v["tv"], v["msg"]
    drel, base, base_i, sel, aggT, fe = v["drel"], v["base"], v["base_i"], v["sel"], v["aggT"], v["fe"]
    hT_ps, hid_ps, xw_ps, agg_ps, out_ps = v["hT_ps"], v["hid_ps"], v["xw_ps"], v["agg_ps"], v["out_ps"]
    edge_rec, long_tab, long_num, ee = v["edge_rec"], v["long_tab"], v["long_num"], v["ee"][layer]
    first = layer == 0
    nfeat = ee.shape[0]
    krad = nfeat + (1 if first else 0)
    hidden = 64 if first else 100
    khid = hidden + (1 if first else 0)
    S1 = RING + 1
    outw = SW if first else MUL0

    def sem(name):
        return lctx.enter_context(nc.semaphore(f"{name}{layer}"))

    win_in = [sem(f"win_in{k}_") for k in range(S1)]
    ee_in = [sem(f"ee_in{k}_") for k in range(S1)]
    xn_in = [sem(f"xn_in{k}_") for k in range(S1)]
    xg_in = [sem(f"xg_in{k}_") for k in range(S1)]
    stored = [sem(f"stored{k}_") for k in range(S1)]
    raw_stats = sem("raw_stats")
    mv_ready = sem("mv_ready")
    ve_ready = sem("ve_ready")
    rs_ready = sem("rs_ready")
    he_ready = sem("he_ready")
    nmr_ready = sem("nmr_ready")
    ra_ready = sem("ra_ready")
    she_ready = sem("she_ready")
    hn_ready = sem("hn_ready")
    xo_ready = sem("xo_ready")
    hT_done = sem("hT_done")
    hT_copied = sem("hT_copied")
    hid_done = sem("hid_done")
    hid_ready = sem("hid_ready")
    xw_done = sem("xw_done")
    xw_copied = sem("xw_copied")
    xs0_ready = sem("xs0_ready")
    pw_ready = sem("pw_ready")
    qv_ready = sem("qv_ready")
    tv_ready = sem("tv_ready")
    msg_ready = sem("msg_ready")
    base_set = sem("base_set")
    drel_ready = sem("drel_ready")
    sel_ready = sem("sel_ready")
    agg_done = sem("agg_done")
    agg_closed = sem("agg_closed")
    aggT_copied = sem("aggT_copied")
    out_done = sem("out_done")
    gates_ready = sem("gates_ready")
    gated_ready = sem("gated_ready")
    rows_ready = sem("rows_ready")
    base_in = sem("base_in")
    passed = sem("passed")

    def second_pass(eng, load, chunk, finish):
        q = eng.alloc_register(f"chunks_before{layer}")
        eng.reg_mov(q, 0)
        n_long = eng.value_load(long_num, min_val=1, max_val=TILES)
        with eng.Fori(0, n_long) as f:
            n_chunks = eng.value_load(long_tab[bass.ds(f, 1), 2:3], min_val=1, max_val=CHUNKS)
            record = load(f)
            with eng.Fori(0, n_chunks) as j:
                before = eng.snap(q, min_val=0, max_val=TILES * CHUNKS)
                chunk(Turn(before + NB, f + NB, before, RING, 0, 1, True), record, j)
                eng.reg_add(q, q, 1)
            done = eng.snap(q, min_val=1, max_val=TILES * CHUNKS)
            finish(Turn(done + (NB - 1), f + NB, done, RING, 0, 1, True), record, f)

    with nc.Block() as block:
        @block.sync
        def _(sp):
            def load_tile(t, j, start):
                sp.dma_start(win[:, t.slot, j, :], edge_rec[bass.ds(start, P), :]).then_inc(win_in[t.slot], 16)
                sp.dma_start(ee_sb[0:nfeat, t.slot, j, :], ee[:, bass.ds(start, P)]).then_inc(ee_in[t.slot], 16)

            def load_waits(t):
                hold(sp, sel_ready, t.freed(RING))
                hold(sp, she_ready, t.freed(RING))
                hold(sp, hid_done, t.freed(RING))
                hold(sp, xo_ready, t.freed(RING))

            def step(T):
                t = T(-2)
                if t:
                    if isinstance(t.n, int):
                        first_edge = [sp.value_load(starts[:, t.n * PAIR + j:t.n * PAIR + j + 1], min_val=0, max_val=EP - P)
                                      for j in range(PAIR)]
                    else:
                        first_edge = group[t.slot]
                    load_waits(t)
                    for j in range(PAIR):
                        load_tile(t, j, first_edge[j])
                    rows = src_rows[bass.ds(t.n * (PAIR * NT), PAIR * NT), :].rearrange("(j p) c -> p j c", p=NT)
                    sp.dma_start(xn[0:NT, t.slot, :, :], rows).then_inc(xn_in[t.slot], 16)
                t = T(6)
                if t:
                    sp.wait_ge(rows_ready, t.m + 1)
                    cols = dst_dram.shape[1]
                    rows = dst_dram[bass.ds(t.n * (PAIR * NT), PAIR * NT), :].rearrange("(j p) c -> p j c", p=NT)
                    sp.dma_start(rows, xo[0:NT, t.slot, :, 0:cols]).then_inc(stored[t.slot], 16)

            group = {}
            regs = [sp.alloc_register(f"first_edge{layer}_{k}") for k in range(RING * PAIR)]

            def load_group(i):
                at = (PEEL + AHEAD) * PAIR
                sp.load(regs, starts[:, bass.ds(i * (RING * PAIR) + at, RING * PAIR)])
                for k in range(RING):
                    group[(PEEL + AHEAD + k) % RING] = [sp.snap(regs[k * PAIR + j], min_val=0, max_val=EP - P) for j in range(PAIR)]

            for s in (-2, -1):
                step(lambda k: main_turn(s - k))
            run_steps(sp, step, load_group)
            for k in range(RING):
                sp.wait_ge(stored[k], 16 * len(range(k, NB, RING)))

            edge = sp.alloc_register(f"edge{layer}")

            def load(f):
                tile = sp.value_load(long_tab[bass.ds(f, 1), 0:1], min_val=0, max_val=TILES - 1)
                start = sp.value_load(long_tab[bass.ds(f, 1), 1:2], min_val=0, max_val=EP - P)
                sp.reg_mov(edge, start)
                sp.wait_ge(sel_ready, NB)
                hold(sp, drel_ready, NB)
                sp.dma_start(base_i[:, :], long_tab[bass.ds(f, 1), 3:4].partition_broadcast(P)).then_inc(base_in, 16)
                return tile, start

            def chunk(t, record, j):
                tile, start = record
                sp.wait_ge(agg_done, t.n)
                load_waits(t)
                load_tile(t, 0, sp.snap(edge, min_val=0, max_val=EP - P))
                sp.reg_add(edge, edge, P)
                sp.dma_start(xn[0:NT, t.slot, 0, :], src_rows[bass.ds(tile * NT, NT), :]).then_inc(xn_in[t.slot], 16)

            def finish(t, record, f):
                sp.wait_ge(rows_ready, t.m + 1)
                cols = dst_dram.shape[1]
                sp.dma_start(dst_dram[bass.ds(record[0] * NT, NT), :], xo[0:NT, t.slot, 0, 0:cols]).then_inc(stored[RING], 16)
                wait_apart(sp, stored[RING], f * 16 + 16, passed)

            second_pass(sp, load, chunk, finish)

        @block.gpsimd
        def _(pool):
            def gather(t):
                wait_apart(pool, win_in[t.slot], (t.uses + 1) * (16 * t.tiles), passed)
                hold(pool, she_ready, t.freed(RING))
                wait_apart(pool, he_ready, t.freed(RING), passed)
                for j in range(t.tiles):
                    pool.indirect_dma_start(out=xg[:, t.slot, j, :], out_offset=None, in_=src_rows,
                                            in_offset=bass.IndirectOffsetOnAxis(ap=win[:, t.slot, j, 0:1], axis=0)
                                            ).then_inc(xg_in[t.slot], 16)

            def rstd(t):
                b = t.tiles
                hold(pool, hn_ready, t.freed(2))
                hold(pool, she_ready, t.freed(2))
                wait_apart(pool, mv_ready, t.n + 1, passed)
                pool.tensor_scalar(ve[:, :, 0:b], mv[:, t.half, :, 0:b, 1], EPS, None, ALU.add).then_inc(ve_ready, 1)
                pool.wait_ge(ve_ready, t.n + 1)
                pool.tensor_tensor(rs[:, t.half, :, 0:b], ve[:, :, 0:b],
                                   neghalf[:, 0:2 * b].rearrange("p (a b) -> p a b", a=2), ALU.pow).then_inc(rs_ready, 1)

            def residual(t):
                b = t.tiles
                if not t.serial:
                    hold(pool, stored[t.slot], t.uses * 16)
                wait_apart(pool, hn_ready, t.n + 1, passed)
                o, a, h = xo[:, t.slot, 0:b, :], xn[:, t.slot, 0:b, :], hn[:, t.half, 0:b, :]
                ins = pool.tensor_tensor(o, a, h, ALU.add) if first else pool.tensor_copy(o, a)
                ins.then_inc(xo_ready, 1)

            def step(T):
                if t := T(2):
                    residual(t)
                if t := T(-1):
                    gather(t)
                if t := T(0):
                    rstd(t)

            step(lambda k: main_turn(-1 - k))
            run_steps(pool, step)

            def chunk(t, record, j):
                gather(t)
                rstd(t)
                residual(t)

            second_pass(pool, lambda f: None, chunk, lambda t, r, f: None)

        @block.vector
        def _(dve):
            def stats(t):
                b = t.tiles
                dve.wait_ge(xg_in[t.slot], (t.uses + 1) * (16 * b))
                dve.wait_ge(xn_in[t.slot], (t.uses + 1) * 16)
                for k, rows in enumerate((xg, xn)):
                    for j in range(b):
                        ins = dve.bn_stats(st[:, t.half, k, j, :], rows[:, t.slot, j, 0:D])
                ins.then_inc(raw_stats, 1)
                hold(dve, rs_ready, t.freed(2))
                wait_apart(dve, raw_stats, t.n + 1, passed)
                for k in range(2):
                    for j in range(b):
                        ins = dve.bn_aggr(mv[:, t.half, k, j, :], st[:, t.half, k, j, :])
                ins.then_inc(mv_ready, 1)
                dve.wait_ge(mv_ready, t.n + 1)
                hold(dve, hT_done, t.freed(2))
                for j in range(b):
                    ins = dve.tensor_scalar(he[:, t.half, j, :], xg[:, t.slot, j, 0:D], mv[:, t.half, 0, j, 0:1], 0.0,
                                            ALU.subtract, ALU.max)
                ins.then_inc(he_ready, 1)

            def scales(t):
                b = t.tiles
                dve.wait_ge(rs_ready, t.n + 1)
                hold(dve, hn_ready, t.freed(2))
                dve.scalar_tensor_tensor(out=nmr[:, t.half, 0:b], in0=mv[:, t.half, 1, 0:b, 0], scalar=-1.0,
                                         in1=rs[:, t.half, 1, 0:b], op0=ALU.mult, op1=ALU.mult).then_inc(nmr_ready, 1)
                r = rs[:, t.half, 0, 0:b]
                if not first:
                    dve.tensor_tensor(ra[:, 0:b], r, xg[:, t.slot, 0:b, D], ALU.mult).then_inc(ra_ready, 1)
                    dve.wait_ge(ra_ready, t.n + 1)
                    r = ra[:, 0:b]
                hold(dve, xs0_ready, t.freed(RING))
                dve.tensor_tensor(she[:, t.slot, 0:b, :], win[:, t.slot, 0:b, 2:REC].bitcast(F32), r.unsqueeze(2).to_broadcast([P, b, 4]),
                                  ALU.mult).then_inc(she_ready, 1)

            def one_hot(t):
                b = t.tiles
                dve.wait_ge(base_set, t.m + 2 if t.serial else t.n + 1)
                dve.tensor_tensor(drel[:, 0:b], win[:, t.slot, 0:b, 1], base[:, 0:b], ALU.subtract).then_inc(drel_ready, 1)
                dve.wait_ge(drel_ready, t.n + 1)
                if not t.serial:
                    dve.tensor_scalar(base[:, :], base[:, :], float(PAIR * NT), None, ALU.add).then_inc(base_set, 1)
                hold(dve, agg_done, t.freed(2))
                for j in range(b):
                    ins = dve.tensor_scalar(sel[:, t.half, j, :], iota_n[:, :], drel[:, j:j + 1], None, ALU.is_equal)
                ins.then_inc(sel_ready, 1)

            def messages(t):
                b = t.tiles
                x_s = xw_sb[:, t.half, 0:b, 0:MUL0]
                x_v = xw_sb[:, t.half, 0:b, MUL0:D].rearrange("p j (c m) -> p j c m", c=3)
                dve.wait_ge(xw_copied, t.n + 1)
                dve.wait_ge(she_ready, t.n + 1)
                x1 = xs0[:, t.half, 0:b, :]
                wt = xw_sb[:, t.half, 0:b, D:D + WN]
                e1 = she[:, t.slot, 0:b, 1:4].unsqueeze(3)
                dve.tensor_tensor(pw[:, 0:b, :], x_s, wt[:, :, MUL0:2 * MUL0], ALU.mult).then_inc(pw_ready, 1)
                dve.tensor_tensor(qv[:, 0:b, :, :], x_v, e1.to_broadcast([P, b, 3, MUL1]), ALU.mult).then_inc(qv_ready, 1)
                hold(dve, agg_done, t.freed(2))
                dve.wait_ge(pw_ready, t.n + 1)
                dve.tensor_tensor(msg[:, t.half, 0:b, 1:4, 0:MUL0], pw[:, 0:b, :].unsqueeze(2).to_broadcast([P, b, 3, MUL0]),
                                  e1.to_broadcast([P, b, 3, MUL0]), ALU.mult)
                dve.wait_ge(qv_ready, t.n + 1)
                dve.tensor_tensor(tv[:, 0, 0:b, :], qv[:, 0:b, 0, :], qv[:, 0:b, 1, :], ALU.add).then_inc(tv_ready, 1)
                dve.wait_ge(xs0_ready, t.n + 1)
                dve.tensor_tensor(msg[:, t.half, 0:b, 0, 0:MUL0], x1[:, :, 0:MUL0], wt[:, :, 0:MUL0], ALU.mult)
                dve.wait_ge(tv_ready, t.n * 2 + 1)
                dve.tensor_tensor(tv[:, 1, 0:b, :], tv[:, 0, 0:b, :], qv[:, 0:b, 2, :], ALU.add).then_inc(tv_ready, 1)
                dve.tensor_tensor(msg[:, t.half, 0:b, 1:4, MUL0:SW], x1[:, :, MUL0:D].rearrange("p j (c m) -> p j c m", c=3),
                                  wt[:, :, 2 * MUL0:2 * MUL0 + MUL1].unsqueeze(2).to_broadcast([P, b, 3, MUL1]), ALU.mult)
                dve.wait_ge(tv_ready, t.n * 2 + 2)
                dve.tensor_tensor(msg[:, t.half, 0:b, 0, MUL0:SW], tv[:, 1, 0:b, :], wt[:, :, WN - MUL1:WN],
                                  ALU.mult).then_inc(msg_ready, 1)

            def new_rows(t):
                b = t.tiles
                if first:
                    g = fe[0:NT, t.half, 0:b, :]
                    dve.wait_ge(gates_ready, t.m + 1)
                    o = out_ps[0:NT, 0:b * 2 * SW].rearrange("p (j c) -> p j c", j=b)
                    dve.tensor_tensor(g[:, :, SW:2 * SW].rearrange("p j (c m) -> p j c m", c=3),
                                      o[:, :, SW:2 * SW].rearrange("p j (c m) -> p j c m", c=3),
                                      g[:, :, 0:MUL1].unsqueeze(2).to_broadcast([NT, b, 3, MUL1]), ALU.mult).then_inc(gated_ready, 1)
                    dve.wait_ge(gated_ready, t.m + 1)
                    dve.wait_ge(xo_ready, t.n + 1)
                    dve.tensor_tensor(xo[0:NT, t.slot, 0:b, :], xo[0:NT, t.slot, 0:b, :], g[:, :, MUL1:2 * SW + 1],
                                      ALU.add).then_inc(rows_ready, 1)
                else:
                    dve.wait_ge(out_done, t.m + 1)
                    dve.wait_ge(xo_ready, t.n + 1)
                    for j in range(b):
                        ins = dve.scalar_tensor_tensor(out=xo[0:NT, t.slot, j, 0:D], in0=out_ps[0:NT, j * 2 * SW:j * 2 * SW + D],
                                                       scalar=xo[0:NT, t.slot, j, D:DA], in1=xo[0:NT, t.slot, j, 0:D],
                                                       op0=ALU.mult, op1=ALU.add)
                    ins.then_inc(rows_ready, 1)

            dve.memset(base[:, 0:1], 0.0)
            dve.memset(base[:, 1:2], float(NT)).then_inc(base_set, 1)

            def step(T):
                if t := T(6):
                    new_rows(t)
                if t := T(3):
                    messages(t)
                if t := T(1):
                    scales(t)
                if t := T(3):
                    one_hot(t)
                if t := T(0):
                    stats(t)

            run_steps(dve, step)

            def load(f):
                dve.wait_ge(base_in, f * 16 + 16)
                dve.tensor_copy(base[:, 0:1], base_i[:, :]).then_inc(base_set, 1)

            def chunk(t, record, j):
                stats(t)
                one_hot(t)
                scales(t)
                messages(t)

            second_pass(dve, load, chunk, lambda t, r, f: new_rows(t))

        @block.scalar
        def _(act):
            def hidden_act(t):
                b = t.tiles
                act.wait_ge(hid_done, t.n + 1)
                hold(act, xw_done, t.freed(2))
                act.activation(hid[0:hidden, t.half, 0:b, :], hid_ps[0:hidden, 0:b * P].rearrange("p (j e) -> p j e", j=b),
                               ACT.Silu if first else ACT.Relu).then_inc(hid_ready, 1)

            def node_h(t):
                act.wait_ge(nmr_ready, t.n + 1)
                hold(act, hT_done, t.freed(2))
                hold(act, xo_ready, t.freed(2))
                for j in range(t.tiles):
                    ins = act.activation(hn[:, t.half, j, 0:D], xn[:, t.slot, j, 0:D], ACT.Relu, bias=nmr[:, t.half, j:j + 1],
                                         scale=rs[:, t.half, 1, j:j + 1])
                ins.then_inc(hn_ready, 1)

            def copy_hT(t):
                b = t.tiles
                act.wait_ge(hT_done, t.n + 1)
                hold(act, out_done, t.freed_m(RING))
                hold(act, xw_done, t.freed(RING))
                act.copy(hT[:, t.slot, 0:b, :, :], hT_ps[0:SW, 0:b, :, :]).then_inc(hT_copied, 1)

            def copy_xw(t):
                b = t.tiles
                act.wait_ge(xw_done, t.n + 1)
                hold(act, msg_ready, t.freed(2))
                act.copy(xw_sb[:, t.half, 0:b, :], xw_ps[:, 0:b, 0:D + WN]).then_inc(xw_copied, 1)
                act.wait_ge(xw_copied, t.n + 1)
                act.wait_ge(she_ready, t.n + 1)
                for j in range(b):
                    ins = act.activation(xs0[:, t.half, j, :], xw_sb[:, t.half, j, 0:D], ACT.Copy, scale=she[:, t.slot, j, 0:1])
                ins.then_inc(xs0_ready, 1)

            def copy_agg(t):
                b = t.tiles
                if t.serial:
                    act.wait_ge(agg_closed, t.m - (NB - 1))
                else:
                    act.wait_ge(agg_done, t.n + 1)
                hold(act, out_done, t.freed_m(2))
                act.copy(aggT[:, t.half, 0:b, :, :], agg_ps[0:SW, 0:b, 0:4 * NT].rearrange("p j (c n) -> p j c n", c=4)
                         ).then_inc(aggT_copied, 1)

            def gates(t):
                if not first:
                    return
                b = t.tiles
                act.wait_ge(out_done, t.m + 1)
                hold(act, rows_ready, t.freed_m(2))
                act.activation(fe[0:NT, t.half, 0:b, 0:SW], out_ps[0:NT, 0:b * 2 * SW].rearrange("p (j c) -> p j c", j=b)[:, :, 0:SW],
                               ACT.Silu).then_inc(gates_ready, 1)

            def step(T):
                if t := T(2):
                    copy_hT(t)
                if t := T(4):
                    copy_agg(t)
                if t := T(1):
                    node_h(t)
                if t := T(5):
                    gates(t)
                if t := T(2):
                    copy_xw(t)
                if t := T(1):
                    hidden_act(t)

            run_steps(act, step)

            def chunk(t, record, j):
                hidden_act(t)
                node_h(t)
                copy_hT(t)
                copy_xw(t)

            def finish(t, record, f):
                copy_agg(t)
                gates(t)

            second_pass(act, lambda f: None, chunk, finish)

        @block.tensor
        def _(pe):
            def transposes(t):
                hold(pe, hT_copied, t.freed(1))
                pe.wait_ge(he_ready, t.n + 1)
                for j in range(t.tiles):
                    pe.transpose(hT_ps[0:SW, j, 0, :], he[:, t.half, j, 0:SW], ident[:, :])
                    pe.transpose(hT_ps[0:SW, j, 1, :], he[:, t.half, j, MUL0:D], ident[:, :])
                pe.wait_ge(hn_ready, t.n + 1)
                for j in range(t.tiles):
                    pe.transpose(hT_ps[0:SW, j, 2, :], hn[:, t.half, j, 0:SW], ident[:, :])
                    ins = pe.transpose(hT_ps[0:SW, j, 3, :], hn[:, t.half, j, MUL0:D], ident[:, :])
                ins.then_inc(hT_done, 1)

            def radial(t):
                pe.wait_ge(ee_in[t.slot], (t.uses + 1) * (16 * t.tiles))
                hold(pe, hid_ready, t.freed(1))
                for j in range(t.tiles):
                    ins = pe.matmul(hid_ps[0:hidden, j * P:(j + 1) * P], w["fc1_"][:, :], ee_sb[0:krad, t.slot, j, :],
                                    start=True, stop=True)
                ins.then_inc(hid_done, 1)

            def edges(t):
                pe.wait_ge(hT_copied, t.n + 1)
                pe.wait_ge(hid_ready, t.n + 1)
                hold(pe, xw_copied, t.freed(1))
                for j in range(t.tiles):
                    pe.matmul(xw_ps[:, j, 0:MUL0], hT[0:MUL0, t.slot, j, 0, :], w["lin_s"][:, :], start=True, stop=True)
                    pe.matmul(xw_ps[:, j, MUL0:D], hT[:, t.slot, j, 1, :], w["lin_v"][:, :], start=True, stop=True)
                    ins = pe.matmul(xw_ps[:, j, D:D + WN], hid[0:khid, t.half, j, :], w["fc2_"][:, :], start=True, stop=True)
                ins.then_inc(xw_done, 1)

            def sums(t):
                pe.wait_ge(msg_ready, t.n + 1)
                pe.wait_ge(sel_ready, t.n + 1)
                if not t.serial:
                    hold(pe, aggT_copied, t.freed_m(1))
                for j in range(t.tiles):
                    for c in range(4):
                        ins = pe.matmul(agg_ps[0:SW, j, c * NT:(c + 1) * NT], msg[:, t.half, j, c, :], sel[:, t.half, j, :],
                                        start=not t.serial, stop=not t.serial, skip_group_check=t.serial)
                ins.then_inc(agg_done, 1)

            def outputs(t):
                pe.wait_ge(aggT_copied, t.m + 1)
                hold(pe, rows_ready, t.freed_m(1))
                for j in range(t.tiles):
                    o = j * 2 * SW
                    pe.matmul(out_ps[0:NT, o:o + outw], hT[0:MUL0, t.slot, j, 2, 0:NT], w["sc_s"][:, :], start=True, stop=True)
                    pe.matmul(out_ps[0:NT, o:o + outw], aggT[:, t.half, j, 0, :], w["out_s"][:, :],
                              start=False, stop=True, skip_group_check=True)
                    pe.matmul(out_ps[0:NT, o + outw:o + outw + VEC], hT[:, t.slot, j, 3, 0:NT], w["sc_v"][:, :],
                              start=False, stop=True, skip_group_check=True)
                    for c in range(3):
                        ins = pe.matmul(out_ps[0:NT, o + outw + c * MUL1:o + outw + (c + 1) * MUL1], aggT[:, t.half, j, 1 + c, :],
                                        w["out_v"][:, :], start=False, stop=True, skip_group_check=True)
                ins.then_inc(out_done, 1)

            def step(T):
                if t := T(4):
                    sums(t)
                if t := T(5):
                    outputs(t)
                if t := T(2):
                    edges(t)
                if t := T(1):
                    radial(t)
                    transposes(t)

            run_steps(pe, step)

            def load(f):
                pe.wait_ge(aggT_copied, f + NB)
                pe.matmul(agg_ps[0:SW, 0, 0:4 * NT], zeros[:, 0:SW], zeros[:, 0:4 * NT], start=True, stop=False, skip_group_check=True)

            def chunk(t, record, j):
                radial(t)
                transposes(t)
                edges(t)
                sums(t)

            def finish(t, record, f):
                pe.matmul(agg_ps[0:SW, 0, 0:4 * NT], zeros[:, 0:SW], zeros[:, 0:4 * NT], start=False, stop=True,
                          skip_group_check=True).then_inc(agg_closed, 1)
                outputs(t)

            second_pass(pe, load, chunk, finish)


def kernel(**inputs):
    import concourse.bacc as bacc
    from concourse.bass_utils import run_bass_kernel_spmd

    a = {k: np.ascontiguousarray(v) for k, v in inputs.items()}
    arrays = {}

    def rows(v):
        return v.reshape(-1, MUL1, 3).transpose(0, 2, 1).reshape(-1, VEC)

    xa = np.zeros((N, DA), np.float32)
    xa[:, :MUL0] = a["x"][:, :MUL0]
    xa[:, MUL0:D] = rows(a["x"][:, MUL0:])
    xa[:, D:] = a["node_vec1"]
    arrays["x"] = xa
    sd = np.zeros((EP, 2), np.int32)
    sd[:, 1] = N
    sd[:E, 0] = a["src"]
    sd[:E, 1] = a["dst"]
    arrays["sd"] = sd
    dst = np.full((EP + 1,), N, np.int32)
    dst[:E] = a["dst"]
    arrays["dst_rows"] = dst[:EP].reshape(P, ROW)
    arrays["dst_next"] = dst[1:].reshape(P, ROW)
    arrays["row_last"] = dst[:EP].reshape(P, ROW)[:, ROW - 1]
    sh = np.zeros((EP, 4), np.float32)
    sh[:E] = a["edge_attr_4"]
    arrays["sh"] = sh
    for layer, name in enumerate(("edge_attr_8", "edge_attr_10")):
        t = np.zeros((a[name].shape[1], EP), np.float32)
        t[:, :E] = a[name].T
        arrays[f"ee{layer}"] = t

    def three(m):
        t = np.zeros((VEC, VEC), np.float32)
        for c in range(3):
            t[c * MUL1:(c + 1) * MUL1, c * MUL1:(c + 1) * MUL1] = m
        return t

    def gates_first(m):
        return np.concatenate([m[:, MUL0:SW], m[:, :MUL0]], axis=1)

    g0 = {k[7:]: v for k, v in a.items() if k.startswith("L0_gnn_")}
    g1 = {k[7:]: v for k, v in a.items() if k.startswith("L1_gnn_")}
    weights = {
        "fc1_0": np.concatenate([g0["fc_w1"], g0["fc_b1"][None]], axis=0),
        "fc2_0": np.concatenate([g0["fc_w2"], g0["fc_b2"][None]], axis=0),
        "lin_s0": g0["W1_s"], "lin_v0": three(g0["W1_v"]),
        "sc_s0": gates_first(g0["Wsc_s"]), "sc_v0": three(g0["Wsc_v"]),
        "out_s0": gates_first(g0["W2_s"]), "out_v0": g0["W2_v"],
        "fc1_1": g1["W_fc1"], "fc2_1": g1["W_fc2"],
        "lin_s1": g1["W_l1_0"], "lin_v1": three(g1["W_l1_1"]),
        "sc_s1": g1["W_si0"], "sc_v1": three(g1["W_si1"]),
        "out_s1": np.concatenate([g1["W_l2_00"], g1["W_l2_10"]], axis=0),
        "out_v1": np.concatenate([g1["W_l2_01"], g1["W_l2_11"]], axis=0),
    }
    arrays.update(weights)
    arrays = {"in_" + k: np.ascontiguousarray(v) for k, v in arrays.items()}

    nc = bacc.Bacc("TRN2", target_bir_lowering=False, num_devices=1)
    ap = {k[3:]: nc.dram_tensor(k, v.shape, mybir.dt.from_np(v.dtype), kind="ExternalInput").ap() for k, v in arrays.items()}
    out = nc.dram_tensor("out", (N, D), F32, kind="ExternalOutput").ap()
    build(nc, ap["x"], ap["sd"], ap["dst_rows"], ap["dst_next"], ap["row_last"], ap["sh"], [ap["ee0"], ap["ee1"]],
          {k: ap[k] for k in weights}, out)
    r = run_bass_kernel_spmd(nc, [arrays], core_ids=[0])
    got = np.asarray(r.results[0]["out"])
    res = np.zeros((N, D), np.float32)
    res[:, :MUL0] = got[:, :MUL0]
    res[:, MUL0:] = got[:, MUL0:].reshape(N, 3, MUL1).transpose(0, 2, 1).reshape(N, VEC)
    return res
```
